# Optimizing a Trainium2 kernel written in Bass

```python
import numpy as np
import jax
import jax.numpy as jnp

def _softmax(x, axis=-1):
    return jax.nn.softmax(x, axis=axis)

def _gelu(x):
    return jax.nn.gelu(x, approximate=True)

def _silu(x):
    return jax.nn.silu(x)

def _sigmoid(x):
    return jax.nn.sigmoid(x)

def _layernorm(x, axis=-1, eps=1e-05):
    m = jnp.mean(x, axis=axis, keepdims=True)
    v = jnp.var(x, axis=axis, keepdims=True)
    return (x - m) / jnp.sqrt(v + eps)

def _scatter_add(tgt, idx, src, axis=0):
    return tgt.at[idx].add(src)

def _segment_sum(src, seg, n):
    return jax.ops.segment_sum(src, seg, n)
kernel_name = 'mk_seq_postln_d1_jaxref_r8_3d1109'

def setup_inputs(seed: int=0):
    np.random.seed(seed)
    _w = jnp.asarray

    def _L0_attn_setup():
        import jax, jax.numpy as jnp
        import numpy as np
        NUM_HEADS = 16
        CHUNK = 64
        RMS_EPS = 1.1920928955078125e-07

        def _forward(x, w_in, w_out):
            B, S, D = x.shape
            H, hd, C = (NUM_HEADS, D // NUM_HEADS, CHUNK)
            proj = x @ w_in.T
            q, k, v, a, g = jnp.split(proj, 5, axis=-1)
            rs = lambda t: t.reshape(B, S, H, hd)
            q, k, v, a, g = map(rs, (q, k, v, a, g))
            q = q * jax.lax.rsqrt(jnp.mean(q * q, axis=-1, keepdims=True) + RMS_EPS)
            k = jnp.tanh(k)
            a = jnp.clip(jax.nn.sigmoid(a + 2.0), 0.6, 0.9995)
            u = k * v
            NC = S // C
            a_r = a.reshape(B, NC, C, H, hd).transpose(1, 0, 2, 3, 4)
            u_r = u.reshape(B, NC, C, H, hd).transpose(1, 0, 2, 3, 4)

            def step(state, au):
                a_c, u_c = au
                prefix = jnp.cumprod(a_c, axis=1)
                acc = jnp.cumsum(u_c / jnp.maximum(prefix, 1e-06), axis=1)
                states = prefix * (state[:, None] + acc)
                return (states[:, -1], states)
            state0 = jnp.zeros((B, H, hd), dtype=jnp.float32)
            _, mem = jax.lax.scan(step, state0, (a_r, u_r))
            memory = mem.transpose(1, 0, 2, 3, 4).reshape(B, S, H, hd)
            gate = jax.nn.sigmoid(g)
            y = gate * (q * memory) + (1.0 - gate) * v
            return y.reshape(B, S, D) @ w_out.T
        key = jax.random.key(seed)
        k1, k2, k3 = jax.random.split(key, 3)
        B, S, D = (2, 512, 256)
        x = jax.random.normal(k1, (B, S, D), dtype=jnp.float32)
        w_in = jax.random.normal(k2, (5 * D, D), dtype=jnp.float32) * 0.02
        w_out = jax.random.normal(k3, (D, D), dtype=jnp.float32) * 0.02
        return {'x': x, 'w_in': w_in, 'w_out': w_out}
    _L0_attn_in = _L0_attn_setup()

    def _L0_ffn_setup():
        import jax, jax.numpy as jnp
        import numpy as np
        B, S, H = (2, 64, 256)
        E, I, K = (64, 176, 6)
        NS = 2
        SH_I = I * NS
        key = jax.random.key(seed)
        ks = jax.random.split(key, 6)
        s = 0.02
        return {'hidden_states': jax.random.normal(ks[0], (B, S, H), jnp.float32), 'gate_w': jax.random.normal(ks[1], (E, H), jnp.float32) * s, 'experts_w1': jax.random.normal(ks[2], (E, I, H), jnp.float32) * s, 'experts_w2': jax.random.normal(ks[3], (E, H, I), jnp.float32) * s, 'shared_gate_up': jax.random.normal(ks[4], (2 * SH_I, H), jnp.float32) * s, 'shared_down': jax.random.normal(ks[5], (H, SH_I), jnp.float32) * s}
    _L0_ffn_in = _L0_ffn_setup()
    _d = {'L0_attn_x': _L0_attn_in['x'], 'L0_attn_w_in': _L0_attn_in['w_in'], 'L0_attn_w_out': _L0_attn_in['w_out'], 'L0_ffn_gate_w': _L0_ffn_in['gate_w'], 'L0_ffn_experts_w1': _L0_ffn_in['experts_w1'], 'L0_ffn_experts_w2': _L0_ffn_in['experts_w2'], 'L0_ffn_shared_gate_up': _L0_ffn_in['shared_gate_up'], 'L0_ffn_shared_down': _L0_ffn_in['shared_down']}
    _x0 = _d['L0_attn_x']
    _d['L0_attn_x'] = jax.random.normal(jax.random.fold_in(jax.random.key(seed), 1), (4, 256, 256), dtype=_x0.dtype)
    del _x0
    return _d

def reference(L0_attn_x, L0_attn_w_in, L0_attn_w_out, L0_ffn_gate_w, L0_ffn_experts_w1, L0_ffn_experts_w2, L0_ffn_shared_gate_up, L0_ffn_shared_down):

    def _L0_attn_ref(x, w_in, w_out):
        import jax, jax.numpy as jnp
        import numpy as np
        NUM_HEADS = 16
        CHUNK = 64
        RMS_EPS = 1.1920928955078125e-07

        def _forward(x, w_in, w_out):
            B, S, D = x.shape
            H, hd, C = (NUM_HEADS, D // NUM_HEADS, CHUNK)
            proj = x @ w_in.T
            q, k, v, a, g = jnp.split(proj, 5, axis=-1)
            rs = lambda t: t.reshape(B, S, H, hd)
            q, k, v, a, g = map(rs, (q, k, v, a, g))
            q = q * jax.lax.rsqrt(jnp.mean(q * q, axis=-1, keepdims=True) + RMS_EPS)
            k = jnp.tanh(k)
            a = jnp.clip(jax.nn.sigmoid(a + 2.0), 0.6, 0.9995)
            u = k * v
            NC = S // C
            a_r = a.reshape(B, NC, C, H, hd).transpose(1, 0, 2, 3, 4)
            u_r = u.reshape(B, NC, C, H, hd).transpose(1, 0, 2, 3, 4)

            def step(state, au):
                a_c, u_c = au
                prefix = jnp.cumprod(a_c, axis=1)
                acc = jnp.cumsum(u_c / jnp.maximum(prefix, 1e-06), axis=1)
                states = prefix * (state[:, None] + acc)
                return (states[:, -1], states)
            state0 = jnp.zeros((B, H, hd), dtype=jnp.float32)
            _, mem = jax.lax.scan(step, state0, (a_r, u_r))
            memory = mem.transpose(1, 0, 2, 3, 4).reshape(B, S, H, hd)
            gate = jax.nn.sigmoid(g)
            y = gate * (q * memory) + (1.0 - gate) * v
            return y.reshape(B, S, D) @ w_out.T
        return _forward(x, w_in, w_out)

    def _L0_ffn_ref(hidden_states, gate_w, experts_w1, experts_w2, shared_gate_up, shared_down):
        import jax, jax.numpy as jnp
        import numpy as np
        B, S, H = (2, 64, 256)
        E, I, K = (64, 176, 6)
        NS = 2
        SH_I = I * NS
        orig_shape = hidden_states.shape
        x = hidden_states.reshape(-1, orig_shape[-1])
        router_logits = x @ gate_w.T
        probs = jax.nn.softmax(router_logits, axis=-1)
        topk_w, topk_idx = jax.lax.top_k(probs, K)
        topk_w = topk_w / jnp.sum(topk_w, axis=-1, keepdims=True)
        combine = jnp.sum(jax.nn.one_hot(topk_idx, E, dtype=x.dtype) * topk_w[..., None], axis=1)
        h = jax.nn.silu(jnp.einsum('th,eih->tei', x, experts_w1))
        y = jnp.einsum('tei,ehi->teh', h, experts_w2)
        routed_out = jnp.einsum('teh,te->th', y, combine)
        gu = x @ shared_gate_up.T
        g, u = jnp.split(gu, 2, axis=-1)
        shared_out = jax.nn.silu(g) * u @ shared_down.T
        return (routed_out + shared_out).reshape(orig_shape)
    x = L0_attn_x
    x = _layernorm(x + _L0_attn_ref(x, L0_attn_w_in, L0_attn_w_out), axis=-1)
    x = _layernorm(x + _L0_ffn_ref(x, L0_ffn_gate_w, L0_ffn_experts_w1, L0_ffn_experts_w2, L0_ffn_shared_gate_up, L0_ffn_shared_down), axis=-1)
    return x

_drawn_inputs = setup_inputs


def setup_inputs(seed=0):
    import zlib

    import numpy as np

    out = dict(_drawn_inputs(seed))
    spreads = {}
    factors = {'L0_ffn_gate_w': 3.082,
     'L0_ffn_experts_w1': 2.815,
     'L0_ffn_experts_w2': 2.81,
     'L0_ffn_shared_gate_up': 2.845,
     'L0_ffn_shared_down': 2.843}
    for name, (base, spread) in spreads.items():
        noise = np.random.default_rng([zlib.crc32(name.encode()), seed]).standard_normal(out[name].shape)
        drawn = base * np.exp(spread * noise) if base else spread * noise
        out[name] = jnp.asarray(drawn.astype(out[name].dtype))
    for name, factor in factors.items():
        out[name] = (out[name] * factor).astype(out[name].dtype)
    return out
```

```python
from contextlib import ExitStack

import concourse.bass as bass
from concourse import mybir

P = 128
F32 = mybir.dt.float32
BF16 = mybir.dt.bfloat16
U32 = mybir.dt.uint32
I32 = mybir.dt.int32
ALU = mybir.AluOpType
ACT = mybir.ActivationFunctionType
AX_X = mybir.AxisListType.X

B, S, D = 4, 256, 256
T = B * S
TT = T // P
TB = S // P
DC = D // P
HEADS, HD, CHUNK = 16, 16, 64
E, I, K = 64, 176, 6
IH = I // 2
SI = 2 * I
SM = [128, 128, 96]
RMS_EPS, LN_EPS = 1.1920928955078125e-07, 1e-5
RMAX = T // P
NTILE = RMAX * E
MT = E
XW = D + E
U = 8
LAG = 6
MAGIC = 12582912.0

C_ID, C_TRI, C_ONE, C_IOTA, C_TOK = 0, 128, 256, 384, 448
C_HS, C_JM, C_TWO, C_EPS, C_RMS, C_PAD = 456, 488, 489, 490, 491, 492
C_HX = C_PAD + P
C_END = C_HX + 2 * P
QA, QK, QV, QQ, QG = 3, 1, 2, 0, 4


def build(nc, x_tok, x_t, w_in, w_out, gate, w1, w2, gu, down, const, out):
    x1_dram = nc.dram_tensor("x1_rows", [T + P, XW], F32).ap()
    table_dram = nc.dram_tensor("slot_tokens", [NTILE, P], F32).ap()
    sum_dram = [nc.dram_tensor(f"sum{i}", [T + P, D], F32).ap() for i in range(2)]

    with ExitStack() as ctx:
        def sb(name, shape, dt=F32):
            return ctx.enter_context(nc.sbuf_tensor(name, shape, dt))

        def sem(name):
            return ctx.enter_context(nc.semaphore(name))

        bank = [ctx.enter_context(nc.psum_tensor(f"bank{i}", [P, 512], F32)) for i in range(8)]

        cst = sb("cst", [P, C_END])
        xtok = sb("xtok", [P, TT, D])
        xT = sb("xT", [P, DC, T])
        win = sb("win", [P, DC, 5 * D])
        wout = sb("wout", [P, DC, D])
        gatew = sb("gatew", [P, DC, E])
        guw = sb("guw", [P, DC, 2 * SI])
        downw = sb("downw", [P, 3, D])
        tri = sb("tri", [P, P], BF16)
        ones = sb("ones", [P, P], BF16)
        zero = sb("zero", [P, NTILE])
        W = DC * S
        shared_mem = sb("shared_mem", [P, max(18 * W, U * (3 * D + I))])
        (av0, av1, kk0, kk1, vv0, vv1, qq0, qq1, gg0, gg1, sq, first, carry, pref, rp, wk, st, yT) = [
            shared_mem[:, i * W:(i + 1) * W] for i in range(18)]
        av, kk, vv, qq, gg = (av0, av1), (kk0, kk1), (vv0, vv1), (qq0, qq1), (gg0, gg1)
        msq = sb("msq", [HEADS, S])
        rsq = sb("rsq", [HEADS, S])
        res = sb("res", [P, TB, D])
        bst = sb("bst", [P, TB, 6])
        mv = sb("mv", [P, TB, 2])
        ve = sb("ve", [P, TB])
        rstd = sb("rstd", [P, TB])
        x1 = sb("x1", [P, TT, D])
        x1T = sb("x1T", [P, DC, T])
        lg = sb("lg", [P, TT, E])
        top = sb("top", [P, TT, 8])
        topi = sb("topi", [P, TT, 8], U32)
        topf = sb("topf", [P, TT, 8])
        oneh = sb("oneh", [P, TB * K, E])
        prod = sb("prod", [P, TB * K, E])
        mask = sb("mask", [P, TT, E], BF16)
        rsel = sb("rsel", [P, TB * K])
        rfl = sb("rfl", [P, TB * K])
        sbase = sb("sbase", [P, TB * K])
        slot = sb("slot", [P, TT * K], U32)
        ex = sb("ex", [P, TT, E])
        den = sb("den", [P, TT])
        rden = sb("rden", [P, TT])
        cw = sb("cw", [P, TT, E])
        fmv = sb("fmv", [P, TT, 2])
        fvar = sb("fvar", [P, TT])
        fstd = sb("fstd", [P, TT])
        cnt = sb("cnt", [P, E])
        over = sb("over", [P, RMAX - 1, E])
        opre = sb("opre", [P, (RMAX - 1) * E])
        olt = sb("olt", [P, (RMAX - 1) * E])
        osum = sb("osum", [P, 1])
        tidf = sb("tidf", [MT, 1])
        tidu = sb("tidu", [MT, 1], U32)
        meta = sb("meta", [1, MT + 1], I32)
        slots = sb("slots", [E, P])
        over_slots = sb("over_slots", [MT, P])
        gidx = sb("gidx", [P, E], U32)
        over_gidx = sb("over_gidx", [P, MT], U32)
        gcur = sb("gcur", [P, 2 * U], U32)
        sg = [sb(f"sg{i}", [P, 512]) for i in range(2)]
        hsh = sb("hsh", [P, 3, T])
        w1r = sb("w1r", [P, U, DC * I])
        w2r = sb("w2r", [IH, U, 2 * D])
        xgT, hT, ysb = [shared_mem[:, i * U * D:(i + 1) * U * D].rearrange("p (u d) -> p u d", u=U)
                        for i in range(3)]
        hs = shared_mem[:, 3 * U * D:3 * U * D + U * I].rearrange("p (u i) -> p u i", u=U)
        xg = sb("xg", [P, U, XW])
        ident = cst[:, C_ID:C_ID + P]

        loaded = [sem(f"loaded{i}") for i in range(9)]
        LX, LXT, LWIN, LWOUT, LGATE, LGU, LDN, LCST, LDN2 = range(9)
        proj_ready = sem("proj_ready")
        evac = sem("evac")
        sumsq_ready = sem("sumsq_ready")
        msq_ready = sem("msq_ready")
        rsq_ready = sem("rsq_ready")
        qscale_ready = sem("qscale_ready")
        qscale_used = sem("qscale_used")
        y_ready = sem("y_ready")
        attn_ready = sem("attn_ready")
        attn_used = sem("attn_used")
        var_ready = sem("var_ready")
        rstd_ready = sem("rstd_ready")
        x1_ready = sem("x1_ready")
        x1_stored = sem("x1_stored")
        x1t_ready = sem("x1t_ready")
        x1t_copied = sem("x1t_copied")
        logit_ready = sem("logit_ready")
        mask_ready = sem("mask_ready")
        rank_ready = sem("rank_ready")
        rank_used = sem("rank_used")
        slot_ready = sem("slot_ready")
        scattered = sem("scattered")
        zero_ready = sem("zero_ready")
        table_zeroed = sem("table_zeroed")
        kv_ready = sem("kv_ready")
        gated_q_ready = sem("gated_q_ready")
        gated_v_ready = sem("gated_v_ready")
        rest_ready = sem("rest_ready")
        tri_ready = sem("tri_ready")
        exp_ready = sem("exp_ready")
        sh_gu_ready = sem("sh_gu_ready")
        sh_silu_ready = sem("sh_silu_ready")
        sh_h_ready = sem("sh_h_ready")
        sh_y_ready = sem("sh_y_ready")
        sh_y_used = sem("sh_y_used")
        cnt_ready = sem("cnt_ready")
        tid_ready = sem("tid_ready")
        trow_ready = sem("trow_ready")
        meta_ready = sem("meta_ready")
        slots_loaded = sem("slots_loaded")
        slots_turned = sem("slots_turned")
        gidx_ready = sem("gidx_ready")
        gcur_ready = sem("gcur_ready")
        pool_turn = sem("pool_turn")
        sp_turn = sem("sp_turn")
        cw_ready = sem("cw_ready")
        cw_stored = sem("cw_stored")
        pads_stored = sem("pads_stored")
        base_stored = sem("base_stored")
        xg_ready = [sem(f"xg_ready{u}") for u in range(U)]
        w_ready = [sem(f"w_ready{u}") for u in range(U)]
        added = [sem(f"added{u}") for u in range(U)]
        over_rows = sem("over_rows")
        over_turned = sem("over_turned")
        over_gidx_ready = sem("over_gidx_ready")
        over_gcur = sem("over_gcur")
        over_w = sem("over_w")
        over_xg = sem("over_xg")
        over_xt = sem("over_xt")
        over_xt_copied = sem("over_xt_copied")
        over_h = sem("over_h")
        over_silu = sem("over_silu")
        over_ht = sem("over_ht")
        over_ht_copied = sem("over_ht_copied")
        over_ymm = sem("over_ymm")
        over_y = sem("over_y")
        over_added = sem("over_added")
        routed_done = sem("routed_done")
        sum_loaded = [sem(f"sum_loaded{b}") for b in range(B)]
        xt_ready = sem("xt_ready")
        xt_copied = sem("xt_copied")
        h_ready = sem("h_ready")
        silu_ready = sem("silu_ready")
        ht_ready = sem("ht_ready")
        ht_copied = sem("ht_copied")
        ymm_ready = sem("ymm_ready")
        y_copied = sem("y_copied")
        fvar_ready = sem("fvar_ready")
        fstd_ready = sem("fstd_ready")
        fin_ready = sem("fin_ready")
        out_stored = sem("out_stored")
        dstep = sem("dstep")

        def wait_from(eng, s, base, off):
            if isinstance(base, int) and base + off <= 0:
                return
            eng.wait_ge(s, base + off)

        block = ctx.enter_context(nc.Block())

        @block.sync
        def _(sp):
            sp.dma_start(xT[:], x_t.rearrange("(c p) t -> p c t", p=P)).then_inc(loaded[LXT], 16)
            sp.dma_start(win[:], w_in.rearrange("(c p) n -> p c n", p=P)).then_inc(loaded[LWIN], 16)
            sp.dma_start(cst[:], const).then_inc(loaded[LCST], 16)
            sp.dma_start(wout[:], w_out.rearrange("(c p) n -> p c n", p=P)).then_inc(loaded[LWOUT], 16)
            sp.dma_start(xtok[:], x_tok.rearrange("(t p) d -> p t d", p=P)).then_inc(loaded[LX], 16)
            sp.dma_start(gatew[:], gate.rearrange("(c p) n -> p c n", p=P)).then_inc(loaded[LGATE], 16)
            sp.wait_ge(loaded[LCST], 16)
            sp.dma_start(table_dram.rearrange("(n p) c -> p n c", p=P),
                         cst[:, None, C_PAD:C_PAD + P].broadcast_to([P, NTILE // P, P])).then_inc(table_zeroed, 16)
            sp.wait_ge(zero_ready, 1)
            sp.dma_start(x1_dram[T:T + P, :], zero[:, 0:XW]).then_inc(pads_stored, 16)
            sp.dma_start(sum_dram[0][T:T + P, :], zero[:, 0:D]).then_inc(pads_stored, 16)
            sp.dma_start(sum_dram[1].rearrange("(n p) d -> p n d", p=P),
                         zero[:, None, 0:D].broadcast_to([P, TT + 1, D])).then_inc(pads_stored, 16)
            sp.dma_start(guw[:], gu.rearrange("(c p) n -> p c n", p=P)).then_inc(loaded[LGU], 16)
            sp.dma_start(downw[:, 0:2, :], down[0:2 * P].rearrange("(c p) n -> p c n", p=P)).then_inc(loaded[LDN], 16)
            sp.dma_start(downw[0:SM[2], 2, :], down[2 * P:SI]).then_inc(loaded[LDN2], 16)

            def load_weights(u, expert):
                sp.dma_start(w1r[:, u, :], w1[bass.ds(expert * P, P), :]).then_inc(w_ready[u], 16)
                sp.dma_start(w2r[:, u, :], w2[bass.ds(expert * IH, IH), :]).then_inc(w_ready[u], 16)

            for j in range(U):
                load_weights(j, j)
            for b in range(B):
                sp.wait_ge(x1_ready, b + 1)
                sp.dma_start(x1_dram[b * S:(b + 1) * S, 0:D].rearrange("(t p) d -> p t d", p=P),
                             x1[:, b * TB:(b + 1) * TB, :]).then_inc(x1_stored, 16)
            sp.wait_ge(cw_ready, 1)
            sp.dma_start(x1_dram[0:T, D:XW].rearrange("(t p) e -> p t e", p=P), cw[:]).then_inc(cw_stored, 16)
            sp.wait_ge(scattered, 16 * TT * K)
            sp.dma_start(slots[:], table_dram[0:E, :]).then_inc(slots_loaded, 16)
            sp.wait_ge(sh_y_used, TT)
            sp.dma_start(sum_dram[0][0:T].rearrange("(t p) d -> p t d", p=P), x1[:]).then_inc(base_stored, 16)

            with sp.Fori(0, E // U - 1) as g:
                for u in range(U):
                    sp.wait_ge(ymm_ready, U * g + u + 1)
                    sp.wait_ge(w_ready[u], 32 * g + 32)
                    load_weights(u, U * g + U + u)

            over = sp.value_load(meta[0:1, MT:MT + 1], min_val=0, max_val=MT)
            with sp.If(over > 0):
                sp.wait_ge(ymm_ready, E)
                with sp.Fori(0, over) as n:
                    tile = sp.value_load(meta[0:1, bass.ds(n, 1)], min_val=E, max_val=NTILE - 1)
                    expert = sp.snap(tile % E)
                    sp.dma_start(w1r[:, 0, :], w1[bass.ds(expert * P, P), :]).then_inc(over_w, 16)
                    sp.dma_start(w2r[:, 0, :], w2[bass.ds(expert * IH, IH), :]).then_inc(over_w, 16)
                    sp.wait_ge(over_added, 16 * n + 16)
                    sp.sem_inc(sp_turn, 1)

            sp.wait_ge(routed_done, 1)
            for b in range(B):
                for dst, src in ((x1, sum_dram[0]), (xtok, sum_dram[1])):
                    sp.dma_start(dst[:, b * TB:(b + 1) * TB, :],
                                 src[b * S:(b + 1) * S].rearrange("(t p) d -> p t d", p=P)).then_inc(sum_loaded[b], 16)
            for t in range(TT):
                sp.wait_ge(fin_ready, t + 1)
                sp.dma_start(out[t * P:(t + 1) * P, :], x1[:, t, :]).then_inc(out_stored, 16)
            sp.wait_ge(out_stored, 16 * TT)

        @block.gpsimd
        def _(pool):
            nc.gpsimd.memset(zero[:], 0.0).then_inc(zero_ready, 1)
            for t in range(B + 3):
                if t < B:
                    i = t % 2
                    pool.wait_ge(evac, 6 * t + 3)
                    nc.gpsimd.tensor_tensor(kk[i], kk[i], vv[i], ALU.mult).then_inc(kv_ready, 1)
                    pool.wait_ge(evac, 6 * t + 6)
                    nc.gpsimd.tensor_tensor(qq[i], qq[i], gg[i], ALU.mult).then_inc(gated_q_ready, 1)
                    pool.wait_ge(gated_q_ready, t + 1)
                    nc.gpsimd.tensor_tensor(gg[i], gg[i], vv[i], ALU.mult).then_inc(gated_v_ready, 1)
                    pool.wait_ge(kv_ready, t + 1)
                    pool.wait_ge(gated_v_ready, t + 1)
                    nc.gpsimd.tensor_tensor(vv[i], vv[i], gg[i], ALU.subtract).then_inc(rest_ready, 1)
                if 0 <= t - 3 < B:
                    b = t - 3
                    pool.wait_ge(slot_ready, b + 1)
                    if b == 0:
                        pool.wait_ge(table_zeroed, 16)
                        pool.wait_ge(loaded[LCST], 16)
                    for n in range(b * TB * K, (b + 1) * TB * K):
                        t_ = n // K
                        nc.gpsimd.indirect_dma_start(
                            table_dram.rearrange("a b -> (a b)").rearrange("(n o) -> n o", o=1),
                            bass.IndirectOffsetOnAxis(ap=slot[:, n:n + 1], axis=0),
                            cst[:, C_TOK + t_:C_TOK + t_ + 1], None).then_inc(scattered, 16)
            pool.wait_ge(gidx_ready, 1)
            pool.wait_ge(x1_stored, 16 * B)
            pool.wait_ge(cw_stored, 16)
            pool.wait_ge(pads_stored, 48)

            def number(g, off):
                if off >= 2 * U:
                    for i in range(4):
                        pool.wait_ge(added[(off + i) % U], 16 * (2 * g + off // U - 1))
                    pool.sem_inc(pool_turn, 1)
                c = off % (2 * U)
                nc.gpsimd.tensor_copy(gcur[:, c:c + 4], gidx[:, bass.ds(2 * U * g + off, 4)]).then_inc(gcur_ready, 1)
                pool.wait_ge(gcur_ready, 2 * U // 4 * g + off // 4 + 1)
                pool.sem_inc(pool_turn, 1)

            def gather(g, off):
                if off % 4 == 0:
                    number(g, off)
                u, c = off % U, off % (2 * U)
                if off >= U:
                    pool.wait_ge(y_copied, 2 * U * g + off - U + 1)
                    pool.sem_inc(pool_turn, 1)
                nc.gpsimd.indirect_dma_start(xg[:, u, :], None, x1_dram,
                                             bass.IndirectOffsetOnAxis(ap=gcur[:, c:c + 1], axis=0)
                                             ).then_inc(xg_ready[u], 16)

            def add(g, off):
                u, c, before = off % U, off % (2 * U), off - 2
                if before >= 0:
                    pool.wait_ge(added[before % U], 16 * (2 * g + before // U + 1))
                pool.wait_ge(y_copied, 2 * U * g + off + 1)
                pool.sem_inc(pool_turn, 1)
                nc.gpsimd.indirect_dma_start(sum_dram[u % 2], bass.IndirectOffsetOnAxis(ap=gcur[:, c:c + 1], axis=0),
                                             ysb[:, u, :], None, compute_op=ALU.add).then_inc(added[u], 16)

            for s in range(2 * U):
                gather(0, s)
                if s == LAG:
                    pool.wait_ge(base_stored, 16)
                if s >= LAG:
                    add(0, s - LAG)
            with pool.Fori(0, E // (2 * U) - 1) as g:
                for s in range(2 * U, 4 * U):
                    gather(g, s)
                    add(g, s - LAG)
            for s in range(E, E + LAG):
                add(E // (2 * U) - 1, s - LAG - (E - 2 * U))
            for u in range(U):
                pool.wait_ge(added[u], 16 * (E // U))

            pool.wait_ge(meta_ready, 2)
            over = pool.value_load(meta[0:1, MT:MT + 1], min_val=0, max_val=MT)
            with pool.If(over > 0):
                nc.gpsimd.indirect_dma_start(over_slots[:], None, table_dram,
                                             bass.IndirectOffsetOnAxis(ap=tidu[:, 0:1], axis=0)).then_inc(over_rows, 16)
                pool.wait_ge(over_gidx_ready, 1)
                with pool.Fori(0, over) as n:
                    nc.gpsimd.tensor_copy(gcur[:, 0:1], over_gidx[:, bass.ds(n, 1)]).then_inc(over_gcur, 1)
                    pool.wait_ge(over_gcur, n + 1)
                    pool.sem_inc(pool_turn, 1)
                    nc.gpsimd.indirect_dma_start(xg[:, 0, :], None, x1_dram,
                                                 bass.IndirectOffsetOnAxis(ap=gcur[:, 0:1], axis=0)).then_inc(over_xg, 16)
                    pool.wait_ge(over_y, n + 1)
                    pool.sem_inc(pool_turn, 1)
                    nc.gpsimd.indirect_dma_start(sum_dram[0], bass.IndirectOffsetOnAxis(ap=gcur[:, 0:1], axis=0),
                                                 ysb[:, 0, :], None, compute_op=ALU.add).then_inc(over_added, 16)
                    pool.wait_ge(over_added, 16 * n + 16)
                    pool.sem_inc(pool_turn, 1)
            pool.sem_inc(routed_done, 1)

        @block.scalar
        def _(act):
            act.wait_ge(loaded[LCST], 16)

            def shared_gate(half):
                for n in range(3 * half, 3 * half + 3):
                    m = SM[n % 3]
                    act.wait_ge(sh_gu_ready, 2 * n + 1)
                    if n >= 2:
                        act.wait_ge(sh_h_ready, n - 1)
                    nc.scalar.activation(sg[n % 2][0:m, :], bank[n % 2][0:m, :], ACT.Silu).then_inc(sh_silu_ready, 1)

            for t in range(B + 2):
                if t < B:
                    i = t % 2
                    if t >= 2:
                        act.wait_ge(y_ready, t - 1)
                    act.wait_ge(proj_ready, 5 * t + 1)
                    nc.scalar.activation(av[i][:], bank[QA][:], ACT.Sigmoid, bias=cst[:, C_TWO:C_TWO + 1]).then_inc(evac, 1)
                    act.wait_ge(proj_ready, 5 * t + 2)
                    nc.scalar.activation(kk[i][:], bank[QK][:], ACT.Tanh).then_inc(evac, 1)
                    act.wait_ge(proj_ready, 5 * t + 3)
                    nc.scalar.activation(vv[i][:], bank[QV][:], ACT.Copy).then_inc(evac, 1)
                    act.wait_ge(proj_ready, 5 * t + 4)
                    if t > 0:
                        act.wait_ge(sumsq_ready, t)
                    nc.scalar.activation(sq, bank[QQ][:], ACT.Square).then_inc(evac, 1)
                    nc.scalar.activation(qq[i][:], bank[QQ][:], ACT.Copy).then_inc(evac, 1)
                    act.wait_ge(proj_ready, 5 * t + 5)
                    nc.scalar.activation(gg[i][:], bank[QG][:], ACT.Sigmoid).then_inc(evac, 1)
                    act.wait_ge(sumsq_ready, t + 1)
                    if t > 0:
                        act.wait_ge(rsq_ready, t)
                    nc.scalar.activation(msq[:], bank[6][0:HEADS, 0:S], ACT.Sqrt,
                                         bias=cst[0:HEADS, C_RMS:C_RMS + 1]).then_inc(msq_ready, 1)
                if 0 <= t - 2 < B:
                    b = t - 2
                    act.wait_ge(x1t_ready, b + 1)
                    nc.scalar.activation(x1T[:, :, b * S:(b + 1) * S],
                                         bank[7][:].rearrange("p (c t) -> p c t", c=DC), ACT.Copy).then_inc(x1t_copied, 1)
                if 0 <= t - 1 < B:
                    act.wait_ge(var_ready, t)
                    if t > 1:
                        act.wait_ge(x1_ready, t - 1)
                    nc.scalar.activation(rstd[:], ve[:], ACT.Sqrt, bias=cst[:, C_EPS:C_EPS + 1]).then_inc(rstd_ready, 1)
                if t == B:
                    shared_gate(0)
            act.wait_ge(mask_ready, B)
            nc.scalar.activation(ex[:], lg[:], ACT.Exp).then_inc(exp_ready, 1)
            shared_gate(1)

            def silu(g, off):
                u = off % U
                act.wait_ge(h_ready, U * g + off + 1)
                wait_from(act, ht_ready, U * g, off - (U - 1))
                nc.scalar.activation(hs[:, u, :], bank[2 + u % 2][:, 0:I], ACT.Silu).then_inc(silu_ready, 1)

            def weigh_y(g, off):
                u = off % U
                if off >= U:
                    act.wait_ge(added[u], 16 * (g + off // U))
                act.wait_ge(ymm_ready, U * g + off + 1)
                nc.scalar.activation(ysb[:, u, :], bank[6 + u % 2][:, 0:D], ACT.Copy,
                                     scale=xg[:, u, bass.ds(U * g + D + off, 1)]).then_inc(y_copied, 1)

            for s in range(2 * U):
                if s >= 1:
                    silu(0, s - 1)
                if s >= 3:
                    weigh_y(0, s - 3)
            with act.Fori(0, E // U - 2) as g:
                for s in range(2 * U, 3 * U):
                    silu(g, s - 1)
                    weigh_y(g, s - 3)
            silu(0, E - 1)
            for s in range(E, E + 3):
                weigh_y(0, s - 3)

            act.wait_ge(meta_ready, 2)
            over = act.value_load(meta[0:1, MT:MT + 1], min_val=0, max_val=MT)
            with act.If(over > 0):
                with act.Fori(0, over) as n:
                    tile = act.value_load(meta[0:1, bass.ds(n, 1)], min_val=E, max_val=NTILE - 1)
                    expert = act.snap(tile % E)
                    act.wait_ge(over_h, n + 1)
                    nc.scalar.activation(hs[:, 0, :], bank[2][:, 0:I], ACT.Silu).then_inc(over_silu, 1)
                    act.wait_ge(over_ymm, n + 1)
                    nc.scalar.activation(ysb[:, 0, :], bank[6][:, 0:D], ACT.Copy,
                                         scale=xg[:, 0, bass.ds(expert + D, 1)]).then_inc(over_y, 1)

            for t in range(TT):
                act.wait_ge(fvar_ready, t + 1)
                nc.scalar.activation(fstd[:, t:t + 1], fvar[:, t:t + 1], ACT.Sqrt,
                                     bias=cst[:, C_EPS:C_EPS + 1]).then_inc(fstd_ready, 1)

        @block.tensor
        def _(pe):
            mm, tp = nc.tensor.matmul, nc.tensor.transpose
            pe.wait_ge(loaded[LXT], 16)
            pe.wait_ge(loaded[LWIN], 16)

            def shared_up(half):
                pe.wait_ge(loaded[LGU], 16)
                pe.wait_ge(evac, 6 * B)
                pe.wait_ge(x1t_copied, B // 2 * (half + 1))
                for n in range(3 * half, 3 * half + 3):
                    m = SM[n % 3]
                    if n >= 2:
                        pe.wait_ge(sh_h_ready, n - 1)
                    for part, bk in ((0, n % 2), (1, 2 + n % 2)):
                        col = part * SI + (n % 3) * P
                        for c in range(DC):
                            last = mm(bank[bk][0:m, :], guw[:, c, col:col + m],
                                      x1T[:, c, half * (T // 2):(half + 1) * (T // 2)],
                                      start=(c == 0), stop=(c == DC - 1))
                        last.then_inc(sh_gu_ready, 1)

            def shared_down(half):
                pe.wait_ge(loaded[LDN], 16)
                pe.wait_ge(loaded[LDN2], 16)
                pe.wait_ge(sh_h_ready, 3 * (half + 1))
                pe.wait_ge(qscale_used, B)
                for t in range(TT // 2 * half, TT // 2 * (half + 1)):
                    bk = 4 if t % 2 == 0 else 6
                    if t >= 2:
                        pe.wait_ge(sh_y_used, t - 1)
                    for n, m in enumerate(SM):
                        last = mm(bank[bk][:, 0:D], hsh[0:m, n, t * P:(t + 1) * P], downw[0:m, n, :],
                                  start=(n == 0), stop=(n == 2))
                    last.then_inc(sh_y_ready, 1)

            for t in range(B + 3):
                if 0 <= t - 3 < B:
                    b = t - 3
                    pe.wait_ge(mask_ready, b + 1)
                    if b == 0:
                        pe.wait_ge(tri_ready, 2)
                    for i in range(TB):
                        tile = b * TB + i
                        o = bank[5][:, 128 + i * E:128 + (i + 1) * E]
                        last = mm(o, tri[:], mask[:, tile, :], start=True, stop=(tile == 0))
                        for k in range(tile):
                            last = mm(o, ones[:], mask[:, k, :], start=False, stop=(k == tile - 1))
                    last.then_inc(rank_ready, 1)
                if t < B:
                    b = t
                    for n, (kind, left) in enumerate([(QA, 1), (QK, 2), (QV, 3), (QQ, 5), (QG, 6)]):
                        if b > 0:
                            pe.wait_ge(evac, 6 * (b - 1) + left)
                        for c2 in range(DC):
                            for c in range(DC):
                                last = mm(bank[kind][:, c2 * S:(c2 + 1) * S],
                                          win[:, c, kind * D + c2 * P:kind * D + (c2 + 1) * P],
                                          xT[:, c, b * S:(b + 1) * S], start=(c == 0), stop=(c == DC - 1))
                        last.then_inc(proj_ready, 1)
                if 0 <= t - 2 < B:
                    b = t - 2
                    pe.wait_ge(x1_ready, b + 1)
                    for i in range(TB):
                        for c in range(DC):
                            last = tp(bank[7][:, c * S + i * P:c * S + (i + 1) * P],
                                      x1[:, b * TB + i, c * P:(c + 1) * P], ident)
                    last.then_inc(x1t_ready, 1)
                if t < B:
                    pe.wait_ge(evac, 6 * t + 4)
                    pe.wait_ge(loaded[LCST], 16)
                    if t > 0:
                        pe.wait_ge(qscale_used, t)
                    for c in range(DC):
                        last = mm(bank[6][0:HEADS, 0:S], cst[:, C_HS + c * HEADS:C_HS + (c + 1) * HEADS],
                                  sq[:, c * S:(c + 1) * S], start=(c == 0), stop=(c == DC - 1))
                    last.then_inc(sumsq_ready, 1)
                if 0 <= t - 1 < B:
                    b = t - 1
                    pe.wait_ge(y_ready, b + 1)
                    pe.wait_ge(loaded[LWOUT], 16)
                    if b > 0:
                        pe.wait_ge(x1t_copied, b)
                    for i in range(TB):
                        for c in range(DC):
                            last = mm(bank[7][:, i * D:(i + 1) * D], yT[:, c * S + i * P:c * S + (i + 1) * P],
                                      wout[:, c, :], start=(c == 0), stop=(c == DC - 1))
                    last.then_inc(attn_ready, 1)
                if 0 <= t - 2 < B:
                    b = t - 2
                    pe.wait_ge(x1t_copied, b + 1)
                    pe.wait_ge(loaded[LGATE], 16)
                    if b > 0:
                        pe.wait_ge(rank_used, b)
                    for i in range(TB):
                        for c in range(DC):
                            last = mm(bank[5][:, i * E:(i + 1) * E],
                                      x1T[:, c, b * S + i * P:b * S + (i + 1) * P],
                                      gatew[:, c, :], start=(c == 0), stop=(c == DC - 1))
                    last.then_inc(logit_ready, 1)
                if t < B:
                    pe.wait_ge(rsq_ready, t + 1)
                    for c in range(DC):
                        last = mm(bank[6][:, c * S:(c + 1) * S], cst[0:HEADS, C_HX + c * P:C_HX + (c + 1) * P],
                                  rsq[:], start=True, stop=True)
                    last.then_inc(qscale_ready, 1)
                if t == B:
                    shared_up(0)
                if t == B + 1:
                    shared_down(0)

            pe.wait_ge(rank_used, B)
            for k in range(TT):
                last = mm(bank[5][:, 0:E], ones[:], mask[:, k, :], start=(k == 0), stop=(k == TT - 1))
            last.then_inc(cnt_ready, 1)
            shared_up(1)
            pe.wait_ge(tid_ready, 2)
            mm(bank[7][0:1, 0:MT], tidf[:, 0:1], cst[0:MT, C_ID:C_ID + MT],
               start=True, stop=True).then_inc(trow_ready, 1)
            pe.wait_ge(slots_loaded, 16)
            pe.wait_ge(meta_ready, 2)
            tp(bank[7][:, 0:E], slots[:], cst[0:E, C_ID:C_ID + E]).then_inc(slots_turned, 1)
            shared_down(1)
            pe.wait_ge(sh_y_used, TT)
            pe.wait_ge(gidx_ready, 1)

            def turn_x(g, off):
                u = off % U
                pe.wait_ge(xg_ready[u], 16 * (g + off // U + 1))
                wait_from(pe, xt_copied, U * g, off - 1)
                for c in range(DC):
                    last = tp(bank[u % 2][:, c * P:(c + 1) * P], xg[:, u, c * P:(c + 1) * P], ident)
                last.then_inc(xt_ready, 1)

            def up(g, off):
                u = off % U
                pe.wait_ge(w_ready[u], 32 * (g + off // U + 1))
                wait_from(pe, silu_ready, U * g, off - 1)
                pe.wait_ge(xt_copied, U * g + off + 1)
                for c in range(DC):
                    last = mm(bank[2 + u % 2][:, 0:I], xgT[:, u, c * P:(c + 1) * P],
                              w1r[:, u, c * I:(c + 1) * I], start=(c == 0), stop=(c == DC - 1))
                last.then_inc(h_ready, 1)

            def turn_h(g, off):
                u = off % U
                wait_from(pe, ht_copied, U * g, off - 1)
                pe.wait_ge(silu_ready, U * g + off + 1)
                for c in range(2):
                    last = tp(bank[4 + u % 2][0:IH, c * P:(c + 1) * P], hs[:, u, c * IH:(c + 1) * IH], ident)
                last.then_inc(ht_ready, 1)

            def down_(g, off):
                u = off % U
                wait_from(pe, y_copied, U * g, off - 1)
                pe.wait_ge(ht_copied, U * g + off + 1)
                for c in range(2):
                    last = mm(bank[6 + u % 2][:, 0:D], hT[0:IH, u, c * P:(c + 1) * P],
                              w2r[:, u, c * D:(c + 1) * D], start=(c == 0), stop=(c == 1))
                last.then_inc(ymm_ready, 1)

            for s in range(2 * U):
                turn_x(0, s)
                if s >= 1:
                    up(0, s - 1)
                if s >= 2:
                    turn_h(0, s - 2)
                if s >= 3:
                    down_(0, s - 3)
            with pe.Fori(0, E // U - 2) as g:
                for s in range(2 * U, 3 * U):
                    turn_x(g, s)
                    up(g, s - 1)
                    turn_h(g, s - 2)
                    down_(g, s - 3)
            up(0, E - 1)
            turn_h(0, E - 2)
            down_(0, E - 3)
            turn_h(0, E - 1)
            down_(0, E - 2)
            down_(0, E - 1)

            over = pe.value_load(meta[0:1, MT:MT + 1], min_val=0, max_val=MT)
            with pe.If(over > 0):
                pe.wait_ge(over_rows, 16)
                pe.wait_ge(y_copied, E)
                tp(bank[7][:, 0:MT], over_slots[:], cst[0:MT, C_ID:C_ID + MT]).then_inc(over_turned, 1)
                with pe.Fori(0, over) as n:
                    pe.wait_ge(over_xg, 16 * n + 16)
                    for c in range(DC):
                        last = tp(bank[0][:, c * P:(c + 1) * P], xg[:, 0, c * P:(c + 1) * P], ident)
                    last.then_inc(over_xt, 1)
                    pe.wait_ge(over_w, 32 * n + 32)
                    pe.wait_ge(over_xt_copied, n + 1)
                    for c in range(DC):
                        last = mm(bank[2][:, 0:I], xgT[:, 0, c * P:(c + 1) * P], w1r[:, 0, c * I:(c + 1) * I],
                                  start=(c == 0), stop=(c == DC - 1))
                    last.then_inc(over_h, 1)
                    pe.wait_ge(over_silu, n + 1)
                    for c in range(2):
                        last = tp(bank[4][0:IH, c * P:(c + 1) * P], hs[:, 0, c * IH:(c + 1) * IH], ident)
                    last.then_inc(over_ht, 1)
                    pe.wait_ge(over_ht_copied, n + 1)
                    for c in range(2):
                        last = mm(bank[6][:, 0:D], hT[0:IH, 0, c * P:(c + 1) * P], w2r[:, 0, c * D:(c + 1) * D],
                                  start=(c == 0), stop=(c == 1))
                    last.then_inc(over_ymm, 1)

        @block.vector
        def _(dve):
            v = nc.vector
            steps = [0]

            def link(ins):
                steps[0] += 1
                ins.then_inc(dstep, 1)
                dve.wait_ge(dstep, steps[0])

            grid = "p (c n s) -> p c n s"
            link(v.memset(first, 0.0))
            link(v.memset(carry, 1.0))
            link(v.memset(carry.rearrange(grid, c=DC, s=CHUNK)[:, :, 0, 0:1], 0.0))
            dve.wait_ge(loaded[LCST], 16)
            v.tensor_copy(tri[:], cst[:, C_TRI:C_TRI + P]).then_inc(tri_ready, 1)
            v.tensor_copy(ones[:], cst[:, C_ONE:C_ONE + P]).then_inc(tri_ready, 1)

            def recurrence(b):
                i = b % 2
                a, kv, rest, gated_q = av[i], kk[i], vv[i], qq[i]
                starts = a[:].rearrange("p (n s) -> p n s", s=CHUNK)[:, :, 0]
                dve.wait_ge(evac, 6 * b + 1)
                link(v.tensor_scalar(a[:], a[:], 0.6, 0.9995, ALU.max, ALU.min))
                link(v.tensor_copy(first.rearrange("p (n s) -> p n s", s=CHUNK)[:, :, 0], starts))
                link(v.memset(starts, 0.0))
                link(v.tensor_tensor_scan(pref, a[:], first, 0.0, ALU.mult, ALU.add))
                link(v.tensor_scalar(rp, pref, 1e-6, None, ALU.max))
                link(v.reciprocal(rp, rp))
                dve.wait_ge(kv_ready, b + 1)
                link(v.tensor_tensor(wk, kv, rp, ALU.mult))
                link(v.tensor_copy(carry.rearrange(grid, c=DC, s=CHUNK)[:, :, 1:, 0],
                                   pref.rearrange(grid, c=DC, s=CHUNK)[:, :, 0:S // CHUNK - 1, CHUNK - 1]))
                link(v.tensor_tensor_scan(st, carry, wk, 0.0, ALU.mult, ALU.add))
                dve.wait_ge(msq_ready, b + 1)
                if b > 0:
                    dve.wait_ge(qscale_ready, b)
                v.reciprocal(rsq[:], msq[:]).then_inc(rsq_ready, 1)
                link(v.tensor_tensor(st, pref, st, ALU.mult))
                dve.wait_ge(gated_q_ready, b + 1)
                dve.wait_ge(qscale_ready, b + 1)
                v.tensor_tensor(wk, gated_q, bank[6][:], ALU.mult).then_inc(qscale_used, 1)
                dve.wait_ge(qscale_used, b + 1)
                link(v.tensor_tensor(wk, wk, st, ALU.mult))
                dve.wait_ge(rest_ready, b + 1)
                if b > 0:
                    dve.wait_ge(attn_ready, b)
                v.tensor_tensor(yT, wk, rest, ALU.add).then_inc(y_ready, 1)

            def norm(b):
                dve.wait_ge(attn_ready, b + 1)
                dve.wait_ge(loaded[LX], 16)
                link(v.tensor_tensor(res[:], bank[7][:].rearrange("p (t d) -> p t d", t=TB),
                                     xtok[:, b * TB:(b + 1) * TB, :], ALU.add))
                for i in range(TB):
                    link(v.bn_stats(bst[:, i, :], res[:, i, :]))
                for i in range(TB):
                    link(v.bn_aggr(mv[:, i, :], bst[:, i, :]))
                v.tensor_copy(ve[:], mv[:, :, 1]).then_inc(var_ready, 1)
                dve.wait_ge(rstd_ready, b + 1)
                link(v.reciprocal(rstd[:], rstd[:]))
                for i in range(TB):
                    ins = v.tensor_scalar(x1[:, b * TB + i, :], res[:, i, :], mv[:, i, 0:1], rstd[:, i:i + 1],
                                          ALU.subtract, ALU.mult)
                    if i < TB - 1:
                        link(ins)
                ins.then_inc(x1_ready, 1)

            def choose(b):
                dve.wait_ge(logit_ready, b + 1)
                t0, t1 = b * TB, (b + 1) * TB
                link(v.tensor_copy(lg[:, t0:t1, :], bank[5][:, 0:TB * E].rearrange("p (t e) -> p t e", t=TB)))
                for t in range(t0, t1):
                    link(v.max(top[:, t, :], lg[:, t, :]))
                for t in range(t0, t1):
                    link(v.max_index(topi[:, t, :], top[:, t, :], lg[:, t, :]))
                link(v.tensor_copy(topf[:, t0:t1, :], topi[:, t0:t1, :]))
                for i, t in enumerate(range(t0, t1)):
                    link(v.tensor_tensor(oneh[:, i * K:(i + 1) * K, :],
                                         cst[:, None, C_IOTA:C_IOTA + E].broadcast_to([P, K, E]),
                                         topf[:, t, 0:K, None].broadcast_to([P, K, E]), ALU.is_equal))
                for i, t in enumerate(range(t0, t1)):
                    link(v.tensor_scalar(lg[:, t, :], lg[:, t, :], top[:, t, 0:1], None, ALU.subtract))
                for t in range(t0, t1):
                    i = t - t0
                    with nc.allow_low_precision(reason="zeros and ones are exact in bfloat16"):
                        ins = v.tensor_reduce(mask[:, t, :], oneh[:, i * K:(i + 1) * K, :].rearrange("p k e -> p e k"),
                                              AX_X, ALU.add)
                    if t < t1 - 1:
                        link(ins)
                ins.then_inc(mask_ready, 1)

            def place(b):
                t0, t1 = b * TB, (b + 1) * TB
                dve.wait_ge(rank_ready, b + 1)
                for i in range(TB):
                    ins = v.tensor_tensor(prod[:, i * K:(i + 1) * K, :], oneh[:, i * K:(i + 1) * K, :],
                                          bank[5][:, None, 128 + i * E:128 + (i + 1) * E].broadcast_to([P, K, E]),
                                          ALU.mult)
                    if i < TB - 1:
                        link(ins)
                ins.then_inc(rank_used, 1)
                dve.wait_ge(rank_used, b + 1)
                link(v.tensor_reduce(rsel[:], prod[:], AX_X, ALU.add))
                link(v.tensor_scalar(rfl[:], rsel[:], 1.0 / P, -63.5 / P, ALU.mult, ALU.add))
                link(v.tensor_scalar(rfl[:], rfl[:], MAGIC, -MAGIC, ALU.add, ALU.add))
                link(v.scalar_tensor_tensor(sbase[:], rfl[:], float((E - 1) * P), rsel[:], ALU.mult, ALU.add))
                v.scalar_tensor_tensor(slot[:, t0 * K:t1 * K].rearrange("p (t k) -> p t k", k=K),
                                       topf[:, t0:t1, 0:K], float(P),
                                       sbase[:].rearrange("p (t k) -> p t k", k=K),
                                       ALU.mult, ALU.add).then_inc(slot_ready, 1)

            def shared_h(half):
                for n in range(3 * half, 3 * half + 3):
                    m = SM[n % 3]
                    dve.wait_ge(sh_gu_ready, 2 * n + 2)
                    dve.wait_ge(sh_silu_ready, n + 1)
                    v.tensor_tensor(hsh[0:m, n % 3, half * (T // 2):(half + 1) * (T // 2)], sg[n % 2][0:m, :],
                                    bank[2 + n % 2][0:m, :], ALU.mult).then_inc(sh_h_ready, 1)

            def add_shared(half):
                dve.wait_ge(x1_stored, 16 * B)
                for t in range(TT // 2 * half, TT // 2 * (half + 1)):
                    dve.wait_ge(sh_y_ready, t + 1)
                    v.tensor_tensor(x1[:, t, :], x1[:, t, :], bank[4 if t % 2 == 0 else 6][:, 0:D],
                                    ALU.add).then_inc(sh_y_used, 1)

            for t in range(B + 3):
                if 0 <= t - 3 < B:
                    place(t - 3)
                if t < B:
                    recurrence(t)
                if 0 <= t - 1 < B:
                    norm(t - 1)
                if 0 <= t - 2 < B:
                    choose(t - 2)
                if t == B:
                    shared_h(0)
                if t == B + 1:
                    add_shared(0)

            dve.wait_ge(exp_ready, 1)
            dve.wait_ge(mask_ready, B)
            link(v.tensor_reduce(den[:], ex[:], AX_X, ALU.add))
            link(v.reciprocal(rden[:], den[:]))
            link(v.tensor_tensor(ex[:], ex[:], rden[:, :, None].broadcast_to([P, TT, E]), ALU.mult))
            link(v.tensor_tensor(ex[:], ex[:], mask[:], ALU.mult))
            link(v.tensor_reduce(den[:], ex[:], AX_X, ALU.add))
            link(v.reciprocal(rden[:], den[:]))
            v.tensor_tensor(cw[:], ex[:], rden[:, :, None].broadcast_to([P, TT, E]), ALU.mult).then_inc(cw_ready, 1)

            dve.wait_ge(cnt_ready, 1)
            link(v.tensor_copy(cnt[:], bank[5][:, 0:E]))
            for r in range(1, RMAX):
                link(v.tensor_scalar(over[:, r - 1, :], cnt[:], float(P * r), None, ALU.is_gt))
            NO = (RMAX - 1) * E
            link(v.tensor_tensor_scan(opre[:], over[:].rearrange("p r e -> p (r e)"), zero[:, 0:NO], 0.0,
                                      ALU.add, ALU.add))
            link(v.tensor_scalar(olt[:], opre[:], cst[:, C_JM:C_JM + 1], None, ALU.is_le))
            link(v.tensor_reduce(osum[:], olt[:], AX_X, ALU.add))
            v.tensor_scalar(tidf[:], osum[0:MT, :], float(E), float(NTILE - 1), ALU.add, ALU.min).then_inc(tid_ready, 1)
            dve.wait_ge(tid_ready, 1)
            v.tensor_copy(tidu[:], tidf[:]).then_inc(tid_ready, 1)
            v.tensor_copy(meta[0:1, MT:MT + 1], opre[0:1, NO - 1:NO]).then_inc(meta_ready, 1)
            shared_h(1)
            dve.wait_ge(trow_ready, 1)
            v.tensor_copy(meta[0:1, 0:MT], bank[7][0:1, 0:MT]).then_inc(meta_ready, 1)
            dve.wait_ge(slots_turned, 1)
            v.tensor_copy(gidx[:], bank[7][:, 0:E]).then_inc(gidx_ready, 1)
            add_shared(1)

            def keep_x(g, off):
                u = off % U
                wait_from(dve, h_ready, U * g, off - (U - 1))
                dve.wait_ge(xt_ready, U * g + off + 1)
                v.tensor_copy(xgT[:, u, :], bank[u % 2][:, 0:D]).then_inc(xt_copied, 1)

            def keep_h(g, off):
                u = off % U
                wait_from(dve, ymm_ready, U * g, off - (U - 1))
                dve.wait_ge(ht_ready, U * g + off + 1)
                v.tensor_copy(hT[0:IH, u, :], bank[4 + u % 2][0:IH, 0:2 * P]).then_inc(ht_copied, 1)

            for s in range(2 * U):
                keep_x(0, s)
                if s >= 2:
                    keep_h(0, s - 2)
            with dve.Fori(0, E // U - 2) as g:
                for s in range(2 * U, 3 * U):
                    keep_x(g, s)
                    keep_h(g, s - 2)
            keep_h(0, E - 2)
            keep_h(0, E - 1)

            dve.wait_ge(meta_ready, 2)
            over_n = dve.value_load(meta[0:1, MT:MT + 1], min_val=0, max_val=MT)
            with dve.If(over_n > 0):
                dve.wait_ge(over_turned, 1)
                v.tensor_copy(over_gidx[:], bank[7][:, 0:MT]).then_inc(over_gidx_ready, 1)
                with dve.Fori(0, over_n) as n:
                    dve.wait_ge(over_xt, n + 1)
                    v.tensor_copy(xgT[:, 0, :], bank[0][:, 0:D]).then_inc(over_xt_copied, 1)
                    dve.wait_ge(over_ht, n + 1)
                    v.tensor_copy(hT[0:IH, 0, :], bank[4][0:IH, 0:2 * P]).then_inc(over_ht_copied, 1)

            def finish(t):
                dve.wait_ge(fstd_ready, t + 1)
                link(v.reciprocal(fstd[:, t:t + 1], fstd[:, t:t + 1]))
                v.tensor_scalar(x1[:, t, :], x1[:, t, :], fmv[:, t, 0:1], fstd[:, t:t + 1],
                                ALU.subtract, ALU.mult).then_inc(fin_ready, 1)

            for t in range(TT):
                if t % TB == 0:
                    dve.wait_ge(sum_loaded[t // TB], 32)
                link(v.tensor_tensor(x1[:, t, :], x1[:, t, :], xtok[:, t, :], ALU.add))
                link(v.bn_stats(bst[:, 0, :], x1[:, t, :]))
                link(v.bn_aggr(fmv[:, t, :], bst[:, 0, :]))
                v.tensor_copy(fvar[:, t:t + 1], fmv[:, t, 1:2]).then_inc(fvar_ready, 1)
                if t > 0:
                    finish(t - 1)
            finish(TT - 1)


def constants():
    import numpy as np
    c = np.zeros((P, C_END), np.float32)
    p = np.arange(P)
    c[:, C_ID:C_ID + P] = np.eye(P)
    c[:, C_TRI:C_TRI + P] = p[:, None] < p[None, :]
    c[:, C_ONE:C_ONE + P] = 1.0
    c[:, C_IOTA:C_IOTA + E] = np.arange(E)
    c[:, C_TOK:C_TOK + TT] = np.arange(TT) * P + p[:, None]
    c[:, C_JM] = p
    c[:, C_PAD:C_PAD + P] = T + p[None, :]
    c[:, C_TWO] = 2.0
    c[:, C_EPS] = LN_EPS
    c[:, C_RMS] = RMS_EPS
    for n in range(DC):
        head = n * (P // HD) + p // HD
        c[p, C_HS + n * HEADS + head] = 1.0 / HD
        c[head, C_HX + n * P + p] = 1.0
    return c


def kernel(**inputs):
    import numpy as np
    import concourse.bacc as bacc
    from concourse.bass_utils import run_bass_kernel_spmd

    nc = bacc.Bacc("TRN2", target_bir_lowering=False, num_devices=1)
    x = np.ascontiguousarray(inputs["L0_attn_x"]).reshape(T, D)
    w1 = np.asarray(inputs["L0_ffn_experts_w1"])
    w2 = np.asarray(inputs["L0_ffn_experts_w2"])
    arrays = {
        "x_tok": x,
        "x_t": x.T,
        "w_in": np.asarray(inputs["L0_attn_w_in"]).T,
        "w_out": np.asarray(inputs["L0_attn_w_out"]).T,
        "gate": np.asarray(inputs["L0_ffn_gate_w"]).T,
        "w1": w1.reshape(E, I, DC, P).transpose(0, 3, 2, 1).reshape(E * P, DC * I),
        "w2": w2.reshape(E, D, 2, IH).transpose(0, 3, 2, 1).reshape(E * IH, 2 * D),
        "gu": np.asarray(inputs["L0_ffn_shared_gate_up"]).T,
        "down": np.asarray(inputs["L0_ffn_shared_down"]).T,
        "const": constants(),
    }
    arrays = {k: np.ascontiguousarray(a) for k, a in arrays.items()}
    aps = [nc.dram_tensor(k, a.shape, F32, kind="ExternalInput").ap() for k, a in arrays.items()]
    out = nc.dram_tensor("out", [T, D], F32, kind="ExternalOutput").ap()
    build(nc, *aps, out)
    r = run_bass_kernel_spmd(nc, [arrays], core_ids=[0])
    return r.results[0]["out"].reshape(B, S, D)
```
